# Optimizing a Trainium2 kernel written in Bass

```python
import numpy as np
import jax
import jax.numpy as jnp

def _softmax(x, axis=-1):
    return jax.nn.softmax(x, axis=axis)

def _gelu(x):
    return jax.nn.gelu(x, approximate=True)

def _silu(x):
    return jax.nn.silu(x)

def _sigmoid(x):
    return jax.nn.sigmoid(x)

def _layernorm(x, axis=-1, eps=1e-05):
    m = jnp.mean(x, axis=axis, keepdims=True)
    v = jnp.var(x, axis=axis, keepdims=True)
    return (x - m) / jnp.sqrt(v + eps)

def _scatter_add(tgt, idx, src, axis=0):
    return tgt.at[idx].add(src)

def _segment_sum(src, seg, n):
    return jax.ops.segment_sum(src, seg, n)
kernel_name = 'mk_adj_resnorm_d1_adj_r2_f5d0a5'

def setup_inputs(seed: int=0):
    np.random.seed(seed)
    _w = jnp.asarray

    def _rec_inputs():
        import jax
        import jax.numpy as jnp
        _gk = jax.random.key(seed)
        x = 7.22e-05 + 1 * jax.random.normal(jax.random.fold_in(_gk, 1), (8, 2048, 128), jnp.float32)
        _a = jax.random.bernoulli(jax.random.fold_in(_gk, 2), 0.00195312, (2048, 2048))
        _a = jnp.logical_or(_a, jnp.swapaxes(_a, -1, -2))
        _a = jnp.logical_or(_a, jnp.eye(2048, dtype=bool))
        _af = _a.astype(jnp.float32)
        _af = _af * jax.random.uniform(jax.random.fold_in(_gk, 3), (2048, 2048), jnp.float32, 0.05, 0.119748)
        adj = _af
        return (x, adj)
    x, adj = _rec_inputs()

    def _L0_gnn_setup():
        import jax, jax.numpy as jnp
        import numpy as np
        B, N, F_IN, F_OUT = (8, 2048, 128, 128)
        key = jax.random.key(seed)
        k1, k2, k3 = jax.random.split(key, 3)
        H = jax.random.normal(k1, (B, N, F_IN), dtype=jnp.float32)
        W = jax.random.normal(k2, (F_IN, F_OUT), dtype=jnp.float32) * (1.0 / np.sqrt(F_IN))
        A = jax.random.normal(k3, (N, N), dtype=jnp.float32) * (1.414 * np.sqrt(2.0 / (N + N)))
        return {'H': H, 'W': W, 'A': A}
    _L0_gnn_all = _L0_gnn_setup()
    _L0_gnn_in = {k: v for k, v in _L0_gnn_all.items() if k in ('W',)}
    del _L0_gnn_all
    return {'x': x, 'adj': adj, 'L0_gnn_W': _L0_gnn_in['W']}

def reference(x, adj, L0_gnn_W):
    import jax
    import jax.numpy as jnp

    def _L0_gnn_ref(H, W, A):
        import jax, jax.numpy as jnp
        import numpy as np
        B, N, F_IN, F_OUT = (8, 2048, 128, 128)
        HW = jnp.einsum('bnf,fo->bno', H, W)
        A_norm = jax.nn.relu((A + A.T) * 0.5)
        D = jnp.sum(A_norm, axis=1)
        D_safe = jnp.where(D > 0, D, 1.0)
        d_inv_sqrt = jnp.where(D > 0, D_safe ** (-0.5), 0.0)
        DAD = d_inv_sqrt[:, None] * A_norm * d_inv_sqrt[None, :]
        L_norm = jnp.eye(N, dtype=H.dtype) - DAD
        out = jnp.einsum('nm,bmo->bno', L_norm, HW)
        return jax.nn.relu(out)
    x = _layernorm(x + _L0_gnn_ref(x, L0_gnn_W, adj), axis=-1)
    return x

_drawn_inputs = setup_inputs


def setup_inputs(seed=0):
    import zlib

    import numpy as np

    out = dict(_drawn_inputs(seed))
    spreads = {}
    factors = {}
    for name, (base, spread) in spreads.items():
        noise = np.random.default_rng([zlib.crc32(name.encode()), seed]).standard_normal(out[name].shape)
        drawn = base * np.exp(spread * noise) if base else spread * noise
        out[name] = jnp.asarray(drawn.astype(out[name].dtype))
    for name, factor in factors.items():
        out[name] = (out[name] * factor).astype(out[name].dtype)
    return out
```

```python
from contextlib import ExitStack

import concourse.bass as bass
from concourse import mybir

F32 = mybir.dt.float32
F16 = mybir.dt.float16
ALU = mybir.AluOpType
ACT = mybir.ActivationFunctionType
AX = mybir.AxisListType
RMAX = bass.bass_isa.ReduceOp.max

P = 128
CH = 4
L_SCALE = 2.0 ** 15
G_TOP = 2.0 ** 14
TINY = 1e-37
EPS = 1e-5


def stage1_steps(B, T):
    shells = [[("a", k, j, min(j + CH, T)) for j in range(k, T, CH)] for k in range(T)]
    batches = [[("x", b * (T // CH) + c) for c in range(T // CH)] for b in range(B)]
    steps = batches[0] + batches[1]
    for k in range(T):
        steps += shells[k]
        if k + 2 < B:
            steps += batches[k + 2]
    return steps


def gnn_resnorm(nc, x, adj, W, out):
    B, N, F = x.shape
    T = N // P
    C = T // CH
    H = 2
    BH = B // H
    assert F == P and BH * F == 512 and T % CH == 0
    NG = B * C
    steps = stage1_steps(B, T)
    a_steps = [s for s in steps if s[0] == "a"]
    last_a = {s[1]: i + 1 for i, s in enumerate(a_steps)}
    NA = len(a_steps)

    x_t = x.rearrange("b (t p) f -> b p t f", p=P)
    x_n = x.rearrange("b (t p) f -> p b t f", p=P)
    out_n = out.rearrange("b (t p) f -> p b t f", p=P)
    adj_t = adj.rearrange("(t p) c -> p t c", p=P)

    with ExitStack() as ctx:
        def sb(name, shape, dt=F32):
            return ctx.enter_context(nc.sbuf_tensor(name, shape, dt))

        def sem(name):
            return ctx.enter_context(nc.semaphore(name))

        S = sb("S", [P, T, N])
        X = sb("X", [P, B, T * F])
        S16 = S[:, :, :].bitcast(F16).rearrange("p t (n s c) -> p t n s c", s=2, c=P)
        X32 = X[:, :, :].rearrange("p b (t f) -> p b t f", f=F)
        G16 = X[:, :, :].bitcast(F16).rearrange("p b (t s f) -> p b t s f", s=2, f=F)
        Wsb = sb("Wsb", [P, F])
        ident = sb("ident", [P, P])
        work = sb("work", [P, 2, CH * P])
        scaled = sb("scaled", [P, 2, CH, P])
        xo = sb("xo", [P, H, BH, F])
        xmax = sb("xmax", [P, B])
        xall = sb("xall", [P, B])
        bound = sb("bound", [P, B])
        gscale = sb("gscale", [P, B])
        gback = sb("gback", [P, B])
        wbound = sb("wbound", [P, 2])
        rowsum = sb("rowsum", [P, T])
        rowsafe = sb("rowsafe", [P, T])
        mhalf = sb("mhalf", [P, T])
        dinv = sb("dinv", [P, T])
        dneg = sb("dneg", [P, T])
        stats = sb("stats", [P, H, BH, 6])
        pairsum = sb("pairsum", [P, H, BH, 2])
        meandiff = sb("meandiff", [P, H, BH])
        diffsq = sb("diffsq", [P, H, BH])
        vareps = sb("vareps", [P, H, BH])
        rstd = sb("rstd", [P, H, BH])
        shift = sb("shift", [P, H, BH])

        bank = [ctx.enter_context(nc.psum_tensor(f"bank{i}", [P, 512], F32)) for i in range(4)]
        high = ctx.enter_context(nc.psum_tensor("high", [P, 4 * 512], F32))
        xT_ps = [high[:, 0:512], high[:, 512:1024]]
        G_ps = [high[:, 1024:1536], high[:, 1536:2048]]
        dB = high
        acc = [bank[0], bank[1]]

        x_in = [sem(f"x_in{b}") for b in range(B)]
        shell_in = [sem(f"shell_in{k}") for k in range(T)]
        w_in = sem("w_in")
        consts = sem("consts")
        absw = sem("absw")
        wsum = sem("wsum")
        wb_ready = sem("wb_ready")
        xmax_ready = sem("xmax_ready")
        xall_ready = sem("xall_ready")
        bound_ready = sem("bound_ready")
        gscale_ready = sem("gscale_ready")
        gback_ready = sem("gback_ready")
        xT_ready = sem("xT_ready")
        xT_copied = sem("xT_copied")
        g_ready = sem("g_ready")
        ghi_done = sem("ghi_done")
        glo_done = sem("glo_done")
        at_ready = sem("at_ready")
        adds_done = sem("adds_done")
        row_done = sem("row_done")
        rs_chain = sem("rs_chain")
        d_ready = sem("d_ready")
        dB_ready = sem("dB_ready")
        scaled_ready = sem("scaled_ready")
        shi_done = sem("shi_done")
        slo_done = sem("slo_done")
        acc_ready = sem("acc_ready")
        acc_read = [sem(f"acc_read{h}") for h in range(H)]
        t_lo = sem("t_lo")
        branch_ready = sem("branch_ready")
        xo_in = [sem(f"xo_in{h}") for h in range(H)]
        r_ready = sem("r_ready")
        stats_done = sem("stats_done")
        pairs_done = sem("pairs_done")
        var_ready = sem("var_ready")
        ve_done = sem("ve_done")
        rstd_done = sem("rstd_done")
        shift_ready = sem("shift_ready")
        out_ready = sem("out_ready")
        stored = [sem(f"stored{h}") for h in range(H)]

        block = ctx.enter_context(nc.Block())

        @block.sync
        def _(sp):
            sp.dma_start(X32[:, 0], x_t[0]).then_inc(x_in[0], 16)
            sp.dma_start(Wsb[:, :], W).then_inc(w_in, 16)
            sp.dma_start(X32[:, 1], x_t[1]).then_inc(x_in[1], 16)
            for k in range(T):
                sp.dma_start(S[:, k, k * P:], adj_t[:, k, k * P:]).then_inc(shell_in[k], 16)
                if k + 1 < T:
                    sp.dma_start(S[:, k + 1:, k * P:(k + 1) * P],
                                 adj_t[:, k + 1:, k * P:(k + 1) * P]).then_inc(shell_in[k], 16)
                if k + 2 < B:
                    sp.dma_start(X32[:, k + 2], x_t[k + 2]).then_inc(x_in[k + 2], 16)
            for h in range(H):
                sp.dma_start(xo[:, h], x_n[:, h * BH:(h + 1) * BH, 0]).then_inc(xo_in[h], 16)

            def store(n, h):
                sp.wait_ge(out_ready, H * n + h + 1)
                sp.dma_start(out_n[:, h * BH:(h + 1) * BH, bass.ds(n, 1)].rearrange("p b t f -> p b (t f)"),
                             xo[:, h]).then_inc(stored[h], 16)

            with sp.Fori(0, T - 1) as n:
                for h in range(H):
                    store(n, h)
                for h in range(H):
                    sp.wait_ge(stored[h], 16 * n + 16)
                    sp.dma_start(xo[:, h], x_n[:, h * BH:(h + 1) * BH, bass.ds(n + 1, 1)].rearrange("p b t f -> p b (t f)"))\
                      .then_inc(xo_in[h], 16)
            for h in range(H):
                store(T - 1, h)
            for h in range(H):
                sp.wait_ge(stored[h], 16 * T)

        @block.gpsimd
        def _(pool):
            pool.memset(ident[:, :], 0.0).then_inc(consts, 1)
            pool.memset(scaled[:, 0, 0, :], 1.0).then_inc(consts, 1)
            pool.memset(mhalf[:, :], -0.5).then_inc(consts, 1)
            pool.wait_ge(consts, 1)
            pool.affine_select(out=ident[:, :], in_=ident[:, :], compare_op=ALU.not_equal, fill=1.0,
                               base=0, pattern=[[-1, P]], channel_multiplier=1).then_inc(consts, 1)
            for b in range(B):
                pool.wait_ge(xmax_ready, b + 1)
                pool.partition_all_reduce(xall[:, b:b + 1], xmax[:, b:b + 1], P, RMAX).then_inc(xall_ready, 1)
                pool.wait_ge(xall_ready, b + 1)
                if b == 0:
                    pool.wait_ge(wb_ready, 1)
                pool.tensor_scalar(bound[:, b:b + 1], xall[:, b:b + 1], wbound[:, 1:2], TINY,
                                   ALU.mult, ALU.max).then_inc(bound_ready, 1)
            pool.wait_ge(bound_ready, B)
            pool.tensor_scalar(gback[:, :], bound[:, :], 1.0 / L_SCALE, 0.0, ALU.mult, ALU.add)\
                .then_inc(gback_ready, 1)
            pool.wait_ge(row_done, T)
            pool.tensor_scalar(rowsafe[:, :], rowsum[:, :], TINY, 1.0, ALU.max, ALU.mult).then_inc(rs_chain, 1)
            pool.wait_ge(rs_chain, 1)
            pool.wait_ge(consts, 4)
            pool.tensor_tensor(dinv[:, :], rowsafe[:, :], mhalf[:, :], ALU.pow).then_inc(d_ready, 1)
            pool.wait_ge(d_ready, 1)
            pool.tensor_scalar(dneg[:, :], dinv[:, :], -L_SCALE, 0.0, ALU.mult, ALU.add).then_inc(d_ready, 1)

            with pool.Fori(0, T) as n:
                for h in range(H):
                    pool.wait_ge(branch_ready, n * H + h + 1)
                    pool.wait_ge(xo_in[h], n * 16 + 16)
                    xr = xo[:, h].rearrange("p b f -> p (b f)")
                    pool.tensor_tensor(xr, work[:, h, :], xr, ALU.add).then_inc(r_ready, 1)
                    pool.wait_ge(var_ready, n * H + h + 1)
                    pool.tensor_tensor(rstd[:, h, :], vareps[:, h, :], mhalf[:, 0:BH], ALU.pow)\
                        .then_inc(rstd_done, 1)

        @block.scalar
        def _(act):
            def x_transposed(g):
                act.wait_ge(xT_ready, g + 1)
                if g >= 2:
                    act.wait_ge(g_ready, g - 1)
                act.copy(work[:, g % 2, :], xT_ps[g % 2]).then_inc(xT_copied, 1)

            def g_hi(g):
                b, c = divmod(g, C)
                act.wait_ge(g_ready, g + 1)
                act.wait_ge(gscale_ready, b + 1)
                act.activation(G16[:, b, c * CH:(c + 1) * CH, 0, :],
                               G_ps[g % 2].rearrange("p (t f) -> p t f", f=F),
                               ACT.Copy, scale=gscale[:, b:b + 1]).then_inc(ghi_done, 1)

            for step in steps:
                if step[0] == "x":
                    g = step[1]
                    x_transposed(g)
                    if g >= 1:
                        g_hi(g - 1)
                    if g == NG - 1:
                        g_hi(g)
                else:
                    _, k, _, j1 = step
                    if j1 == T:
                        act.wait_ge(adds_done, last_a[k])
                        act.activation(S[:, k, :], S[:, k, :], ACT.Relu,
                                       accum_out=rowsum[:, k:k + 1]).then_inc(row_done, 1)

            def s_hi(n, c):
                act.wait_ge(scaled_ready, n * C + c + 1)
                act.copy(S16[:, c * CH:(c + 1) * CH, bass.ds(n, 1), 0, :].rearrange("p t n c -> p t (n c)"),
                         scaled[:, c % 2]).then_inc(shi_done, 1)

            def normalize(n, h):
                act.wait_ge(shift_ready, n * H + h + 1)
                for b in range(BH):
                    last = act.activation(xo[:, h, b, :], xo[:, h, b, :], ACT.Identity,
                                          scale=rstd[:, h, b:b + 1], bias=shift[:, h, b:b + 1])
                last.then_inc(out_ready, 1)

            for c in range(C):
                s_hi(0, c)
            with act.Fori(0, T - 1) as n:
                for c in range(C):
                    s_hi(n + 1, c)
                for h in range(H):
                    normalize(n, h)
            for h in range(H):
                normalize(T - 1, h)

        @block.vector
        def _(dve):
            dve.wait_ge(w_in, 16)
            dve.scalar_tensor_tensor(out=scaled[:, 0, 1, :], in0=Wsb[:, :], scalar=-1.0, in1=Wsb[:, :],
                                     op0=ALU.mult, op1=ALU.max).then_inc(absw, 1)
            dve.wait_ge(wsum, 1)
            dve.tensor_reduce(wbound[:, 0:1], G_ps[1][:, 0:F], AX.X, ALU.max).then_inc(absw, 1)
            dve.wait_ge(absw, 2)
            dve.tensor_scalar(wbound[:, 1:2], wbound[:, 0:1], 1.0 / G_TOP, None, ALU.mult).then_inc(wb_ready, 1)

            def x_absmax(b):
                dve.wait_ge(x_in[b], 16)
                dve.tensor_reduce(xmax[:, b:b + 1], X[:, b, :], AX.X, ALU.max,
                                  apply_absolute_value=True).then_inc(xmax_ready, 1)

            def g_scale(b):
                dve.wait_ge(bound_ready, b + 1)
                dve.reciprocal(gscale[:, b:b + 1], bound[:, b:b + 1]).then_inc(gscale_ready, 1)

            def g_lo(g):
                b, c = divmod(g, C)
                dve.wait_ge(ghi_done, g + 1)
                dve.wait_ge(gscale_ready, b + 1)
                dve.scalar_tensor_tensor(out=G16[:, b, c * CH:(c + 1) * CH, 1, :],
                                         in0=G_ps[g % 2].rearrange("p (t f) -> p t f", f=F),
                                         scalar=gscale[:, b:b + 1],
                                         in1=G16[:, b, c * CH:(c + 1) * CH, 0, :],
                                         op0=ALU.mult, op1=ALU.subtract).then_inc(glo_done, 1)

            x_absmax(0)
            na = 0
            for step in steps:
                if step[0] == "x":
                    g = step[1]
                    if g % C == 0:
                        b = g // C
                        if b + 1 < B:
                            x_absmax(b + 1)
                    if g >= 1:
                        if (g - 1) % C == 0:
                            g_scale((g - 1) // C)
                        g_lo(g - 1)
                    if g == NG - 1:
                        g_lo(g)
                else:
                    _, k, j0, j1 = step
                    pair = 2 * (na % 2)
                    na += 1
                    dve.wait_ge(at_ready, na)
                    row = S[:, k, j0 * P:j1 * P]
                    last = dve.tensor_tensor(row, row, bank[pair][:, 0:(j1 - j0) * P], ALU.add)
                    i0 = max(j0, k + 1)
                    if i0 < j1:
                        col = S[:, i0:j1, k * P:(k + 1) * P]
                        last = dve.tensor_tensor(
                            col, col, bank[pair + 1][:, (i0 - j0) * P:(j1 - j0) * P]
                            .rearrange("p (t c) -> p t c", c=P), ALU.add)
                    last.then_inc(adds_done, 1)

            def s_scale(n, c, first):
                if c >= 2 or not first:
                    dve.wait_ge(slo_done, n * C + (c - 1))
                for i in range(CH):
                    m = c * CH + i
                    last = dve.scalar_tensor_tensor(out=scaled[:, c % 2, i, :], in0=S[:, m, bass.ts(n, P)],
                                                    scalar=dneg[:, m:m + 1], in1=dB[:, bass.ts(n, P)],
                                                    op0=ALU.mult, op1=ALU.mult)
                last.then_inc(scaled_ready, 1)

            def s_lo(n, c):
                dve.wait_ge(shi_done, n * C + c + 1)
                tiles = S16[:, c * CH:(c + 1) * CH, bass.ds(n, 1), :, :].rearrange("p t n s c -> p t (n s) c")
                dve.tensor_tensor(tiles[:, :, 1, :], scaled[:, c % 2], tiles[:, :, 0, :], ALU.subtract)\
                   .then_inc(slo_done, 1)

            def s_split(n, first=False):
                for c in range(C):
                    s_scale(n, c, first)
                    if c:
                        s_lo(n, c - 1)
                s_lo(n, C - 1)

            def finish(n, h):
                i = n * H + h
                t = work[:, h, :]
                tb = t.rearrange("p (b f) -> p b f", f=F)
                Gn = G16[:, h * BH:(h + 1) * BH, bass.ds(n, 1), :, :].rearrange("p b t s f -> p b (t s) f")
                dve.wait_ge(acc_ready, i + 1)
                dve.scalar_tensor_tensor(out=tb, in0=Gn[:, :, 0, :], scalar=L_SCALE,
                                         in1=acc[h][:, :].rearrange("p (b f) -> p b f", f=F),
                                         op0=ALU.mult, op1=ALU.add).then_inc(acc_read[h], 1)
                dve.wait_ge(acc_read[h], n + 1)
                dve.scalar_tensor_tensor(out=tb, in0=Gn[:, :, 1, :], scalar=L_SCALE, in1=tb,
                                         op0=ALU.mult, op1=ALU.add).then_inc(t_lo, 1)
                dve.wait_ge(t_lo, i + 1)
                back = gback[:, h * BH:(h + 1) * BH].rearrange("p (b o) -> p b o", o=1).broadcast_to([P, BH, F])
                dve.scalar_tensor_tensor(out=tb, in0=tb, scalar=0.0, in1=back,
                                         op0=ALU.max, op1=ALU.mult).then_inc(branch_ready, 1)
                dve.wait_ge(r_ready, i + 1)
                for b in range(BH):
                    last = dve.bn_stats(stats[:, h, b, :], xo[:, h, b, :])
                last.then_inc(stats_done, 1)
                dve.wait_ge(stats_done, i + 1)
                dve.tensor_tensor(pairsum[:, h], stats[:, h, :, 1:3], stats[:, h, :, 4:6], ALU.add)
                dve.tensor_tensor(meandiff[:, h, :], stats[:, h, :, 1], stats[:, h, :, 4], ALU.subtract)\
                   .then_inc(pairs_done, 1)
                dve.wait_ge(pairs_done, i + 1)
                dve.scalar_tensor_tensor(out=diffsq[:, h, :], in0=meandiff[:, h, :], scalar=0.25,
                                         in1=meandiff[:, h, :], op0=ALU.mult, op1=ALU.mult)
                dve.tensor_scalar(vareps[:, h, :], pairsum[:, h, :, 1], 1.0 / F, EPS, ALU.mult, ALU.add)\
                   .then_inc(ve_done, 1)
                dve.wait_ge(ve_done, i + 1)
                dve.tensor_tensor(vareps[:, h, :], vareps[:, h, :], diffsq[:, h, :], ALU.add)\
                   .then_inc(var_ready, 1)
                dve.wait_ge(rstd_done, i + 1)
                dve.scalar_tensor_tensor(out=shift[:, h, :], in0=pairsum[:, h, :, 0], scalar=-0.5,
                                         in1=rstd[:, h, :], op0=ALU.mult, op1=ALU.mult).then_inc(shift_ready, 1)

            dve.wait_ge(d_ready, 2)
            dve.wait_ge(dB_ready, 1)
            dve.wait_ge(gback_ready, 1)
            s_split(0, first=True)
            with dve.Fori(0, T - 1) as n:
                s_split(n + 1)
                for h in range(H):
                    finish(n, h)
            for h in range(H):
                finish(T - 1, h)

        @block.tensor
        def _(pe):
            pe.wait_ge(consts, 4)
            pe.wait_ge(absw, 1)
            pe.matmul(G_ps[1][:, 0:F], scaled[:, 0, 0, :], scaled[:, 0, 1, :], start=True, stop=True)\
              .then_inc(wsum, 1)

            def x_transposes(g):
                b, c = divmod(g, C)
                if c == 0:
                    pe.wait_ge(x_in[b], 16)
                if g >= 2:
                    pe.wait_ge(xT_copied, g - 1)
                for i in range(CH):
                    last = pe.transpose(xT_ps[g % 2][:, i * P:(i + 1) * P], X32[:, b, c * CH + i, :], ident[:, :])
                last.then_inc(xT_ready, 1)

            def x_times_w(g):
                pe.wait_ge(xT_copied, g + 1)
                if g == 1:
                    pe.wait_ge(wb_ready, 1)
                if g >= 2:
                    pe.wait_ge(glo_done, g - 1)
                for i in range(CH):
                    last = pe.matmul(G_ps[g % 2][:, i * F:(i + 1) * F], work[:, g % 2, i * P:(i + 1) * P],
                                     Wsb[:, :], start=True, stop=True)
                last.then_inc(g_ready, 1)

            na = 0
            for step in steps:
                if step[0] == "x":
                    g = step[1]
                    x_transposes(g)
                    if g >= 1:
                        x_times_w(g - 1)
                    if g == NG - 1:
                        x_times_w(g)
                else:
                    _, k, j0, j1 = step
                    pair = 2 * (na % 2)
                    if j0 == k:
                        pe.wait_ge(shell_in[k], 32 if k + 1 < T else 16)
                    if na >= 2:
                        pe.wait_ge(adds_done, na - 1)
                    na += 1
                    for j in range(j0, j1):
                        at = slice((j - j0) * P, (j - j0 + 1) * P)
                        last = pe.transpose(bank[pair][:, at], S[:, j, k * P:(k + 1) * P], ident[:, :])
                        if j > k:
                            last = pe.transpose(bank[pair + 1][:, at], S[:, k, j * P:(j + 1) * P], ident[:, :])
                    last.then_inc(at_ready, 1)

            pe.wait_ge(d_ready, 1)
            pe.wait_ge(glo_done, NG)
            for n in range(T):
                last = pe.transpose(dB[:, n * P:(n + 1) * P], dinv[:, n:n + 1].broadcast_to([P, P]), ident[:, :])
            last.then_inc(dB_ready, 1)
            pe.wait_ge(adds_done, NA)

            def products(n, first=False):
                for h in range(H):
                    if not first:
                        pe.wait_ge(acc_read[h], n)
                    for m in range(T):
                        if h == 0 and m % CH == 0:
                            pe.wait_ge(slo_done, n * C + (m // CH + 1))
                        Lm = S16[:, m, bass.ds(n, 1), :, :].rearrange("p n s c -> p (n s) c")
                        Gm = G16[:, h * BH:(h + 1) * BH, m, :, :]
                        for i, (ls, gs) in enumerate(((0, 0), (0, 1), (1, 0))):
                            last = pe.matmul(acc[h][:, :], Lm[:, ls, :], Gm[:, :, gs, :],
                                             start=(m == 0 and i == 0), stop=(m == T - 1 and i == 2))
                    last.then_inc(acc_ready, 1)

            products(0, first=True)
            with pe.Fori(1, T) as n:
                products(n)


def kernel(x, adj, L0_gnn_W):
    import numpy as np
    import concourse.bacc as bacc
    from concourse.bass_utils import run_bass_kernel_spmd

    nc = bacc.Bacc("TRN2", target_bir_lowering=False, num_devices=1)
    arrays, aps = {}, []
    for name, a in (("x", x), ("adj", adj), ("W", L0_gnn_W)):
        a = np.ascontiguousarray(a)
        arrays[f"in_{name}"] = a
        aps.append(nc.dram_tensor(f"in_{name}", a.shape, mybir.dt.from_np(a.dtype), kind="ExternalInput").ap())
    out = nc.dram_tensor("out", x.shape, F32, kind="ExternalOutput").ap()
    gnn_resnorm(nc, *aps, out)
    result = run_bass_kernel_spmd(nc, [arrays], core_ids=[0])
    return result.results[0]["out"]
```

```python
from contextlib import ExitStack

import concourse.bass as bass
from concourse import mybir

F32 = mybir.dt.float32
F16 = mybir.dt.float16
ALU = mybir.AluOpType
ACT = mybir.ActivationFunctionType
AX = mybir.AxisListType
RMAX = bass.bass_isa.ReduceOp.max

P = 128
CH = 4
L_SCALE = 2.0 ** 15
G_TOP = 2.0 ** 14
TINY = 1e-37
TINY_SQ = 1e-30
EPS = 1e-5


def stage1_steps(B, T):
    shells = [[("a", k, j, min(j + CH, T)) for j in range(k, T, CH)] for k in range(T)]
    batches = [[("x", b * (T // CH) + c) for c in range(T // CH)] for b in range(B)]
    steps = batches[0] + batches[1]
    for k in range(T):
        batch = batches[k + 2] if k + 2 < B else []
        for i in range(max(len(batch), len(shells[k]))):
            steps += shells[k][i:i + 1] + batch[i:i + 1]
        steps.append(("r", k))
    return steps


def relu_parts(k, T):
    half, late = T // 2, 3 * T // 4
    done = [(k, 0, T, 0)] if k < half else [(k, half, T, 1)] if k < late else [(k, late, T, 2)]
    first = {half - 1: half, half: half + 2, late - 1: late, late: late + 2}.get(k)
    if first:
        done += [(row, 0, half, 0) for row in (first, first + 1)]
    if k == late - 1:
        done += [(row, half, late, 1) for row in range(late, T)]
    return done


def copy_on_dve(g):
    return g % 4 == 1


def copies_up_to(g):
    return sum(copy_on_dve(i) == copy_on_dve(g) for i in range(g + 1))


def relu_on_dve(part, row, T):
    return part >= 1 and row >= 3 * T // 4


def gnn_resnorm(nc, x, adj, W, out):
    B, N, F = x.shape
    T = N // P
    C = T // CH
    H = 2
    BH = B // H
    assert F == P and BH * F == 512 and T % CH == 0
    NG = B * C
    XD = 2
    R = 3
    steps = stage1_steps(B, T)
    a_steps = [s for s in steps if s[0] == "a"]
    pair_of, pair_free, free = [], [], {0: 0, 1: 0}
    for i, step in enumerate(steps):
        if step[0] == "a":
            pair = len(pair_of) % 2 if ("x", NG - 1) in steps[:i] else 0
            pair_of.append(pair)
            pair_free.append(free[pair])
            free[pair] = len(pair_of)
    last_a = {s[1]: i + 1 for i, s in enumerate(a_steps)}
    NA = len(a_steps)
    relus = [part for k in range(T) for part in relu_parts(k, T) if not relu_on_dve(part[3], part[0], T)]
    group_relus = [1 + max(i for i, part in enumerate(relus) if part[0] // CH == c) for c in range(C)]
    chain_at = [sum(1 + (c * CH >= T // 2) + (c * CH >= 3 * T // 4) for c in range(n)) for n in range(C + 1)]

    x_t = x.rearrange("b (t p) f -> b p t f", p=P)
    x_n = x.rearrange("b (t p) f -> p b t f", p=P)
    out_n = out.rearrange("b (t p) f -> p b t f", p=P)
    adj_t = adj.rearrange("(t p) c -> p t c", p=P)

    with ExitStack() as ctx:
        def sb(name, shape, dt=F32):
            return ctx.enter_context(nc.sbuf_tensor(name, shape, dt))

        def sem(name):
            return ctx.enter_context(nc.semaphore(name))

        S = sb("S", [P, T, N])
        X = sb("X", [P, B, T * F])
        S16 = S[:, :, :].bitcast(F16).rearrange("p t (n s c) -> p t n s c", s=2, c=P)
        X32 = X[:, :, :].rearrange("p b (t f) -> p b t f", f=F)
        G16 = X[:, :, :].bitcast(F16).rearrange("p b (t s f) -> p b t s f", s=2, f=F)
        Wsb = sb("Wsb", [P, F])
        ident = sb("ident", [P, P])
        work = sb("work", [P, 2, CH * P])
        scaled = sb("scaled", [P, 2, CH, P])
        xo = sb("xo", [P, H, BH, F])
        Wsq = xo[:, 0, 0, :]
        ones = xo[:, 0, 1, :]
        squares = scaled[:, 0].rearrange("p b c -> p (b c)").bitcast(mybir.dt.bfloat16)
        xss = sb("xss", [P, 2, B])
        xss_sum = sb("xss_sum", [P, B])
        xall = sb("xall", [P, B])
        bound = sb("bound", [P, B])
        gscale = sb("gscale", [P, B])
        gback = sb("gback", [P, B])
        wbound = sb("wbound", [P, 2])
        rowsum = sb("rowsum", [P, 3, T])
        rowsafe = sb("rowsafe", [P, T])
        mhalf = sb("mhalf", [P, T])
        phalf = sb("phalf", [P, B])
        dinv = sb("dinv", [P, T])
        dneg = sb("dneg", [P, T])
        stats = sb("stats", [P, H, BH, 6])
        pairsum = sb("pairsum", [P, H, BH, 2])
        meandiff = sb("meandiff", [P, H, BH])
        diffsq = sb("diffsq", [P, H, BH])
        vareps = sb("vareps", [P, H, BH])
        negmean = sb("negmean", [P, H, BH])
        rstd = sb("rstd", [P, H, BH])
        shift = sb("shift", [P, H, BH])

        psum = ctx.enter_context(nc.psum_tensor("psum", [P, 8 * 512], F32))
        bank = [psum[:, i * 512:(i + 1) * 512] for i in range(8)]
        xT_ps = bank[0:R]
        G_ps = bank[R:2 * R]
        at_ps = [bank[6:8], bank[2:4]]
        dB = psum[:, 0:T * P]
        acc = [bank[4], bank[5]]
        xT_sb = [work[:, 0, :], work[:, 1, :], scaled[:, 1].rearrange("p a b -> p (a b)")]

        x0_in = [sem(f"x0_in{c}") for c in range(C)]
        x_in = [None] + [sem(f"x_in{b}") for b in range(1, B)]
        shell_in = [sem(f"shell_in{k}") for k in range(T)]
        w_in = sem("w_in")
        consts = sem("consts")
        wsq_done = sem("wsq_done")
        wsum = sem("wsum")
        wb_ready = sem("wb_ready")
        xss_ready = sem("xss_ready")
        xss_sum_ready = sem("xss_sum_ready")
        xall_ready = sem("xall_ready")
        bound_ready = sem("bound_ready")
        gscale_ready = sem("gscale_ready")
        groot_ready = sem("groot_ready")
        gback_ready = sem("gback_ready")
        xT_ready = sem("xT_ready")
        xT_copied = {False: sem("xT_copied_act"), True: sem("xT_copied_dve")}
        g_ready = sem("g_ready")
        ghi_done = sem("ghi_done")
        glo_done = sem("glo_done")
        at_ready = sem("at_ready")
        adds_done = sem("adds_done")
        relu_act = sem("relu_act")
        relu_dve = sem("relu_dve")
        rs_chain = sem("rs_chain")
        rowsafe_ready = sem("rowsafe_ready")
        d_ready = sem("d_ready")
        dneg_ready = sem("dneg_ready")
        dB_ready = sem("dB_ready")
        scaled_ready = sem("scaled_ready")
        shi_done = sem("shi_done")
        slo_done = sem("slo_done")
        acc_ready = sem("acc_ready")
        acc_read = [sem(f"acc_read{h}") for h in range(H)]
        gn_ready = sem("gn_ready")
        branch_ready = sem("branch_ready")
        xo_in = [sem(f"xo_in{h}") for h in range(H)]
        r_ready = sem("r_ready")
        stats_done = sem("stats_done")
        pairs_done = sem("pairs_done")
        var_ready = sem("var_ready")
        ve_done = sem("ve_done")
        rstd_done = sem("rstd_done")
        shift_ready = sem("shift_ready")
        part_out = sem("part_out")
        out_ready = sem("out_ready")
        stored = [sem(f"stored{h}") for h in range(H)]

        block = ctx.enter_context(nc.Block())

        def squares_inputs(eng, b, half):
            for s in x0_in[half * C // 2:(half + 1) * C // 2] if b == 0 else [x_in[b]]:
                eng.wait_ge(s, 16)
            if 2 * b + half:
                eng.wait_ge(xss_ready, 2 * b + half)
            return X[:, b, half * T // 2 * F:(half + 1) * T // 2 * F]

        @block.sync
        def _(sp):
            for c in range(C):
                sp.dma_start(X32[:, 0, c * CH:(c + 1) * CH], x_t[0][:, c * CH:(c + 1) * CH])\
                  .then_inc(x0_in[c], 16)
                if c == 0:
                    sp.dma_start(Wsb[:, :], W).then_inc(w_in, 16)
            sp.dma_start(X32[:, 1], x_t[1]).then_inc(x_in[1], 16)
            for k in range(T):
                sp.dma_start(S[:, k, k * P:], adj_t[:, k, k * P:]).then_inc(shell_in[k], 16)
                if k + 1 < T:
                    sp.dma_start(S[:, k + 1:, k * P:(k + 1) * P],
                                 adj_t[:, k + 1:, k * P:(k + 1) * P]).then_inc(shell_in[k], 16)
                if k + 2 < B:
                    sp.dma_start(X32[:, k + 2], x_t[k + 2]).then_inc(x_in[k + 2], 16)
            sp.wait_ge(wb_ready, 1)
            for h in range(H):
                sp.dma_start(xo[:, h], x_n[:, h * BH:(h + 1) * BH, 0]).then_inc(xo_in[h], 16)

            def store(n, h):
                sp.wait_ge(out_ready, H * n + h + 1)
                sp.dma_start(out_n[:, h * BH:(h + 1) * BH, bass.ds(n, 1)].rearrange("p b t f -> p b (t f)"),
                             xo[:, h]).then_inc(stored[h], 16)

            with sp.Fori(0, T - 1) as n:
                for h in range(H):
                    store(n, h)
                for h in range(H):
                    sp.wait_ge(stored[h], 16 * n + 16)
                    sp.dma_start(xo[:, h], x_n[:, h * BH:(h + 1) * BH, bass.ds(n + 1, 1)].rearrange("p b t f -> p b (t f)"))\
                      .then_inc(xo_in[h], 16)
            store(T - 1, 0)
            sp.wait_ge(part_out, 1)
            store(T - 1, 1)
            for h in range(H):
                sp.wait_ge(stored[h], 16 * T)

        @block.gpsimd
        def _(pool):
            pool.memset(ident[:, :], 0.0).then_inc(consts, 1)
            pool.memset(ones, 1.0).then_inc(consts, 1)
            pool.memset(mhalf[:, :], -0.5).then_inc(consts, 1)
            pool.memset(phalf[:, :], 0.5).then_inc(consts, 1)
            pool.wait_ge(consts, 1)
            pool.affine_select(out=ident[:, :], in_=ident[:, :], compare_op=ALU.not_equal, fill=1.0,
                               base=0, pattern=[[-1, P]], channel_multiplier=1).then_inc(consts, 1)
            pool.wait_ge(consts, 5)

            def batch_bound(b):
                pool.wait_ge(xss_ready, 2 * b + 2)
                pool.tensor_tensor(xss_sum[:, b:b + 1], xss[:, 0, b:b + 1], xss[:, 1, b:b + 1], ALU.add)\
                    .then_inc(xss_sum_ready, 1)
                pool.wait_ge(xss_sum_ready, b + 1)
                pool.partition_all_reduce(xall[:, b:b + 1], xss_sum[:, b:b + 1], P, RMAX).then_inc(xall_ready, 1)
                pool.wait_ge(xall_ready, b + 1)
                if b == 0:
                    pool.wait_ge(wb_ready, 1)
                pool.tensor_scalar(bound[:, b:b + 1], xall[:, b:b + 1], wbound[:, 1:2], TINY_SQ,
                                   ALU.mult, ALU.max).then_inc(bound_ready, 1)
                pool.wait_ge(bound_ready, b + 1)
                pool.tensor_tensor(gscale[:, b:b + 1], bound[:, b:b + 1], mhalf[:, 0:1], ALU.pow)\
                    .then_inc(gscale_ready, 1)

            def row_scales(c):
                g = slice(c * CH, (c + 1) * CH)
                late = (c + 1) * CH > 3 * T // 4
                pool.wait_ge(relu_act, group_relus[c])
                pool.tensor_scalar(rowsafe[:, g], rowsum[:, 0, g], TINY, 1.0, ALU.add, ALU.mult)\
                    .then_inc(rs_chain, 1)
                for part in range(1, 1 + (c * CH >= T // 2) + late):
                    pool.wait_ge(rs_chain, chain_at[c] + part)
                    if late:
                        pool.wait_ge(relu_dve, CH * part)
                    pool.tensor_tensor(rowsafe[:, g], rowsafe[:, g], rowsum[:, part, g], ALU.add)\
                        .then_inc(rs_chain, 1)
                pool.wait_ge(rs_chain, chain_at[c + 1])
                pool.tensor_tensor(dinv[:, g], rowsafe[:, g], mhalf[:, 0:CH], ALU.pow).then_inc(d_ready, 1)
                pool.wait_ge(d_ready, c + 1)
                pool.tensor_scalar(dneg[:, g], dinv[:, g], -L_SCALE, 0.0, ALU.mult, ALU.add)\
                    .then_inc(dneg_ready, 1)

            for b in range(B):
                batch_bound(b)
            pool.tensor_tensor(gback[:, :], bound[:, :], phalf[:, :], ALU.pow).then_inc(groot_ready, 1)
            pool.wait_ge(groot_ready, 1)
            pool.tensor_scalar(gback[:, :], gback[:, :], 1.0 / L_SCALE, 0.0, ALU.mult, ALU.add)\
                .then_inc(gback_ready, 1)
            for c in range(C):
                row_scales(c)

            with pool.Fori(0, T) as n:
                for h in range(H):
                    pool.wait_ge(var_ready, n * H + h + 1)
                    pool.tensor_tensor(rstd[:, h, :], vareps[:, h, :], mhalf[:, 0:BH], ALU.pow)\
                        .then_inc(rstd_done, 1)
                    pool.wait_ge(rstd_done, n * H + h + 1)
                    pool.tensor_tensor(shift[:, h, :], negmean[:, h, :], rstd[:, h, :], ALU.mult)\
                        .then_inc(shift_ready, 1)

        @block.scalar
        def _(act):
            def x_transposed(g):
                act.wait_ge(xT_ready, g + 1)
                if g >= R:
                    act.wait_ge(g_ready, g - R + 1)
                act.copy(xT_sb[g % R], xT_ps[g % R]).then_inc(xT_copied[False], 1)

            def x_squares(b, half):
                x_half = squares_inputs(act, b, half)
                act.activation(squares, x_half, ACT.Square, accum_out=xss[:, half, b:b + 1])\
                   .then_inc(xss_ready, 1)

            def g_hi(g):
                b, c = divmod(g, C)
                act.wait_ge(g_ready, g + 1)
                act.wait_ge(gscale_ready, b + 1)
                act.activation(G16[:, b, c * CH:(c + 1) * CH, 0, :],
                               G_ps[g % R].rearrange("p (t f) -> p t f", f=F),
                               ACT.Copy, scale=gscale[:, b:b + 1]).then_inc(ghi_done, 1)

            def s_hi(n, c):
                act.wait_ge(scaled_ready, n * C + c + 1)
                act.copy(S16[:, c * CH:(c + 1) * CH, bass.ds(n, 1), 0, :].rearrange("p t n c -> p t (n c)"),
                         scaled[:, c % 2]).then_inc(shi_done, 1)

            hi_at = {T // 2 - 1: 0, T // 2: 1}
            hi_after = {T - 4: 2, T - 1: 3}
            for step in steps:
                if step[0] == "x":
                    g = step[1]
                    if not copy_on_dve(g):
                        x_transposed(g)
                    if g >= 1:
                        g_hi(g - 1)
                    if g % C in (1, 2) and XD <= g // C + 1 < B:
                        x_squares(g // C + 1, g % C - 1)
                    if g == NG - 1:
                        g_hi(g)
                elif step[0] == "r":
                    act.wait_ge(adds_done, last_a[step[1]])
                    for i, (row, j0, j1, part) in enumerate(relu_parts(step[1], T)):
                        if i == 1 and step[1] in hi_at:
                            s_hi(0, hi_at[step[1]])
                        if not relu_on_dve(part, row, T):
                            act.activation(S[:, row, j0 * P:j1 * P], S[:, row, j0 * P:j1 * P], ACT.Relu,
                                           accum_out=rowsum[:, part, row:row + 1]).then_inc(relu_act, 1)
                    if step[1] in hi_after:
                        s_hi(0, hi_after[step[1]])

            def normalize(n, h):
                act.wait_ge(shift_ready, n * H + h + 1)
                for b in range(BH):
                    last = act.activation(xo[:, h, b, :], xo[:, h, b, :], ACT.Identity,
                                          scale=rstd[:, h, b:b + 1], bias=shift[:, h, b:b + 1])
                last.then_inc(out_ready, 1)

            with act.Fori(0, T - 1) as n:
                for c in range(C):
                    s_hi(n + 1, c)
                for h in range(H):
                    normalize(n, h)
            normalize(T - 1, 0)
            act.wait_ge(shift_ready, T * H)
            for b in range(BH // 2):
                last = act.activation(xo[:, 1, b, :], xo[:, 1, b, :], ACT.Identity,
                                      scale=rstd[:, 1, b:b + 1], bias=shift[:, 1, b:b + 1])
            last.then_inc(out_ready, 1)

        @block.vector
        def _(dve):
            dve.wait_ge(w_in, 16)
            dve.tensor_tensor(Wsq, Wsb[:, :], Wsb[:, :], ALU.mult).then_inc(wsq_done, 1)
            dve.wait_ge(wsum, 1)
            dve.tensor_reduce(wbound[:, 0:1], G_ps[2][:, 0:F], AX.X, ALU.max).then_inc(wsq_done, 1)
            dve.wait_ge(wsq_done, 2)
            dve.tensor_scalar(wbound[:, 1:2], wbound[:, 0:1], G_TOP ** -2, None, ALU.mult).then_inc(wb_ready, 1)

            def x_transposed(g):
                dve.wait_ge(xT_ready, g + 1)
                if g >= R:
                    dve.wait_ge(g_ready, g - R + 1)
                dve.tensor_copy(xT_sb[g % R], xT_ps[g % R]).then_inc(xT_copied[True], 1)

            def x_squares(b, half):
                x_half = squares_inputs(dve, b, half)
                dve.scalar_tensor_tensor(out=squares, in0=x_half, scalar=1.0, in1=x_half,
                                         op0=ALU.mult, op1=ALU.mult,
                                         accum_out=xss[:, half, b:b + 1]).then_inc(xss_ready, 1)

            def g_lo(g):
                b, c = divmod(g, C)
                dve.wait_ge(ghi_done, g + 1)
                dve.wait_ge(gscale_ready, b + 1)
                dve.scalar_tensor_tensor(out=G16[:, b, c * CH:(c + 1) * CH, 1, :],
                                         in0=G_ps[g % R].rearrange("p (t f) -> p t f", f=F),
                                         scalar=gscale[:, b:b + 1],
                                         in1=G16[:, b, c * CH:(c + 1) * CH, 0, :],
                                         op0=ALU.mult, op1=ALU.subtract).then_inc(glo_done, 1)

            def s_scale(n, c, first):
                if first:
                    dve.wait_ge(d_ready, c + 1)
                    dve.wait_ge(dB_ready, 1)
                if c >= 2 or not first:
                    dve.wait_ge(slo_done, n * C + (c - 1))
                for i in range(CH):
                    m = c * CH + i
                    last = dve.scalar_tensor_tensor(out=scaled[:, c % 2, i, :], in0=S[:, m, bass.ts(n, P)],
                                                    scalar=dinv[:, m:m + 1], in1=dB[:, bass.ts(n, P)],
                                                    op0=ALU.mult, op1=ALU.mult)
                last.then_inc(scaled_ready, 1)

            def s_lo(n, c):
                dve.wait_ge(shi_done, n * C + c + 1)
                tiles = S16[:, c * CH:(c + 1) * CH, bass.ds(n, 1), :, :].rearrange("p t n s c -> p t (n s) c")
                dve.tensor_tensor(tiles[:, :, 1, :], scaled[:, c % 2], tiles[:, :, 0, :], ALU.subtract)\
                   .then_inc(slo_done, 1)

            def s_split(n):
                for c in range(C):
                    s_scale(n, c, first=False)
                    if c:
                        s_lo(n, c - 1)
                s_lo(n, C - 1)

            scale_after = {T // 2 - 1: 0, T // 2: 1, T - 4: 2, T - 1: 3}
            lo_after = {T // 2: 0, T // 2 + 1: 1, T - 3: 2}
            na = 0
            for step in steps:
                if step[0] == "x":
                    g = step[1]
                    if g >= 2:
                        g_lo(g - 2)
                    if copy_on_dve(g):
                        x_transposed(g)
                    if g % 2 == 0 and g < 2 * XD:
                        for half in range(2):
                            x_squares(g // 2, half)
                    if g == NG - 1:
                        g_lo(g - 1)
                        g_lo(g)
                elif step[0] == "r":
                    k = step[1]
                    for row, j0, j1, part in relu_parts(k, T):
                        if relu_on_dve(part, row, T):
                            dve.wait_ge(adds_done, last_a[k])
                            tiles = S[:, row, j0 * P:j1 * P]
                            dve.scalar_tensor_tensor(out=tiles, in0=tiles, scalar=0.0, in1=tiles,
                                                     op0=ALU.max, op1=ALU.max,
                                                     accum_out=rowsum[:, part, row:row + 1]).then_inc(relu_dve, 1)
                    if k in lo_after:
                        s_lo(0, lo_after[k])
                    if k in scale_after:
                        s_scale(0, scale_after[k], first=True)
                else:
                    _, k, j0, j1 = step
                    pair = at_ps[pair_of[na]]
                    na += 1
                    dve.wait_ge(at_ready, na)
                    row = S[:, k, j0 * P:j1 * P]
                    last = dve.tensor_tensor(row, row, pair[0][:, 0:(j1 - j0) * P], ALU.add)
                    i0 = max(j0, k + 1)
                    if i0 < j1:
                        col = S[:, i0:j1, k * P:(k + 1) * P]
                        last = dve.tensor_tensor(
                            col, col, pair[1][:, (i0 - j0) * P:(j1 - j0) * P]
                            .rearrange("p (t c) -> p t c", c=P), ALU.add)
                    last.then_inc(adds_done, 1)

            def gather(n, h):
                i = n * H + h
                t = work[:, h, :].rearrange("p (b f) -> p b f", f=F)
                Gn = G16[:, h * BH:(h + 1) * BH, bass.ds(n, 1), :, :].rearrange("p b t s f -> p b (t s) f")
                dve.tensor_tensor(t, Gn[:, :, 0, :], Gn[:, :, 1, :], ALU.add).then_inc(gn_ready, 1)
                dve.wait_ge(gn_ready, i + 1)
                dve.wait_ge(acc_ready, i + 1)
                dve.scalar_tensor_tensor(out=t, in0=t, scalar=L_SCALE,
                                         in1=acc[h].rearrange("p (b f) -> p b f", f=F),
                                         op0=ALU.mult, op1=ALU.add).then_inc(acc_read[h], 1)

            def statistics(n, h):
                i = n * H + h
                t = work[:, h, :].rearrange("p (b f) -> p b f", f=F)
                dve.wait_ge(acc_read[h], n + 1)
                back = gback[:, h * BH:(h + 1) * BH].rearrange("p (b o) -> p b o", o=1).broadcast_to([P, BH, F])
                dve.scalar_tensor_tensor(out=t, in0=t, scalar=0.0, in1=back,
                                         op0=ALU.max, op1=ALU.mult).then_inc(branch_ready, 1)
                dve.wait_ge(branch_ready, i + 1)
                dve.wait_ge(xo_in[h], n * 16 + 16)
                dve.tensor_tensor(xo[:, h], t, xo[:, h], ALU.add).then_inc(r_ready, 1)
                dve.wait_ge(r_ready, i + 1)
                for b in range(BH):
                    last = dve.bn_stats(stats[:, h, b, :], xo[:, h, b, :])
                last.then_inc(stats_done, 1)
                dve.wait_ge(stats_done, i + 1)
                dve.tensor_tensor(pairsum[:, h], stats[:, h, :, 1:3], stats[:, h, :, 4:6], ALU.add)
                dve.tensor_tensor(meandiff[:, h, :], stats[:, h, :, 1], stats[:, h, :, 4], ALU.subtract)\
                   .then_inc(pairs_done, 1)
                dve.wait_ge(pairs_done, i + 1)
                dve.scalar_tensor_tensor(out=diffsq[:, h, :], in0=meandiff[:, h, :], scalar=0.25,
                                         in1=meandiff[:, h, :], op0=ALU.mult, op1=ALU.mult)
                dve.tensor_scalar(vareps[:, h, :], pairsum[:, h, :, 1], 1.0 / F, EPS, ALU.mult, ALU.add)\
                   .then_inc(ve_done, 1)
                dve.tensor_scalar(negmean[:, h, :], pairsum[:, h, :, 0], -0.5, None, ALU.mult)
                dve.wait_ge(ve_done, i + 1)
                dve.tensor_tensor(vareps[:, h, :], vareps[:, h, :], diffsq[:, h, :], ALU.add)\
                   .then_inc(var_ready, 1)

            s_lo(0, C - 1)
            for c in range(C):
                s_scale(1, c, first=False)
                if c:
                    s_lo(1, c - 1)
                if c >= C - H:
                    gather(0, c - (C - H))
            s_lo(1, C - 1)
            dve.wait_ge(gback_ready, 1)
            for h in range(H):
                statistics(0, h)
            dve.wait_ge(dB_ready, C)
            with dve.Fori(1, T - 1) as n:
                s_split(n + 1)
                for h in range(H):
                    gather(n, h)
                    statistics(n, h)
            for h in range(H):
                gather(T - 1, h)
                statistics(T - 1, h)
            dve.wait_ge(shift_ready, T * H)
            for b in range(BH // 2, BH):
                last = dve.tensor_scalar(xo[:, 1, b, :], xo[:, 1, b, :], rstd[:, 1, b:b + 1],
                                         shift[:, 1, b:b + 1], ALU.mult, ALU.add)
            last.then_inc(part_out, 1)

        @block.tensor
        def _(pe):
            pe.wait_ge(consts, 5)
            pe.wait_ge(wsq_done, 1)
            pe.matmul(G_ps[2][:, 0:F], ones, Wsq, start=True, stop=True)\
              .then_inc(wsum, 1)

            def x_transposes(g):
                b, c = divmod(g, C)
                if b == 0:
                    pe.wait_ge(x0_in[c], 16)
                elif c == 0:
                    pe.wait_ge(x_in[b], 16)
                if g >= R:
                    pe.wait_ge(xT_copied[copy_on_dve(g - R)], copies_up_to(g - R))
                for i in range(CH):
                    last = pe.transpose(xT_ps[g % R][:, i * P:(i + 1) * P], X32[:, b, c * CH + i, :], ident[:, :])
                last.then_inc(xT_ready, 1)

            def x_times_w(g):
                pe.wait_ge(xT_copied[copy_on_dve(g)], copies_up_to(g))
                if g == 2:
                    pe.wait_ge(wb_ready, 1)
                if g >= R:
                    pe.wait_ge(glo_done, g - R + 1)
                for i in range(CH):
                    last = pe.matmul(G_ps[g % R][:, i * F:(i + 1) * F], xT_sb[g % R][:, i * P:(i + 1) * P],
                                     Wsb[:, :], start=True, stop=True)
                last.then_inc(g_ready, 1)

            def d_columns(c):
                pe.wait_ge(dneg_ready, c + 1)
                if c == 0:
                    pe.wait_ge(glo_done, NG)
                if c == 2:
                    pe.wait_ge(adds_done, NA)
                for n in range(c * CH, (c + 1) * CH):
                    last = pe.transpose(dB[:, n * P:(n + 1) * P], dneg[:, n:n + 1].broadcast_to([P, P]), ident[:, :])
                last.then_inc(dB_ready, 1)

            def three_products(n, m, h):
                Lm = S16[:, m, bass.ds(n, 1), :, :].rearrange("p n s c -> p (n s) c")
                Gm = G16[:, h * BH:(h + 1) * BH, m, :, :]
                for i, (ls, gs) in enumerate(((0, 0), (0, 1), (1, 0))):
                    last = pe.matmul(acc[h], Lm[:, ls, :], Gm[:, :, gs, :],
                                     start=(m == 0 and i == 0), stop=(m == T - 1 and i == 2))
                if m == T - 1:
                    last.then_inc(acc_ready, 1)

            def first_products(m):
                if m % CH == 0:
                    pe.wait_ge(slo_done, m // CH + 1)
                for h in range(H):
                    three_products(0, m, h)

            first_from = [9] * 8 + [T] * 8
            early = list(range(T))
            dB_after = {T // 2 - 2: 0, T // 2 + 1: 1}
            na = 0
            for step in steps:
                if step[0] == "x":
                    g = step[1]
                    x_transposes(g)
                    if g >= 1:
                        x_times_w(g - 1)
                    if g == NG - 1:
                        x_times_w(g)
                elif step[0] == "r":
                    if step[1] in dB_after:
                        d_columns(dB_after[step[1]])
                else:
                    _, k, j0, j1 = step
                    pair = at_ps[pair_of[na]]
                    if j0 == k:
                        pe.wait_ge(shell_in[k], 32 if k + 1 < T else 16)
                    if pair_free[na]:
                        pe.wait_ge(adds_done, pair_free[na])
                    if pair_of[na] == 1:
                        pe.wait_ge(glo_done, NG)
                    na += 1
                    for j in range(j0, j1):
                        at = slice((j - j0) * P, (j - j0 + 1) * P)
                        last = pe.transpose(pair[0][:, at], S[:, j, k * P:(k + 1) * P], ident[:, :])
                        if j > k:
                            last = pe.transpose(pair[1][:, at], S[:, k, j * P:(j + 1) * P], ident[:, :])
                    last.then_inc(at_ready, 1)
                    if k >= first_from[T - len(early)]:
                        first_products(early.pop(0))

            while len(early) > CH:
                first_products(early.pop(0))
            d_columns(2)
            d_columns(3)
            pe.wait_ge(slo_done, C)
            for h in range(H):
                for m in early:
                    three_products(0, m, h)
            assert C == 4

            def products(n):
                for h in range(H):
                    pe.wait_ge(acc_read[h], n)
                    for m in range(T):
                        if h == 0 and m % CH == 0:
                            pe.wait_ge(slo_done, n * C + (m // CH + 1))
                        three_products(n, m, h)

            with pe.Fori(1, T) as n:
                products(n)


def kernel(x, adj, L0_gnn_W):
    import numpy as np
    import concourse.bacc as bacc
    from concourse.bass_utils import run_bass_kernel_spmd

    nc = bacc.Bacc("TRN2", target_bir_lowering=False, num_devices=1)
    arrays, aps = {}, []
    for name, a in (("x", x), ("adj", adj), ("W", L0_gnn_W)):
        a = np.ascontiguousarray(a)
        arrays[f"in_{name}"] = a
        aps.append(nc.dram_tensor(f"in_{name}", a.shape, mybir.dt.from_np(a.dtype), kind="ExternalInput").ap())
    out = nc.dram_tensor("out", x.shape, F32, kind="ExternalOutput").ap()
    gnn_resnorm(nc, *aps, out)
    result = run_bass_kernel_spmd(nc, [arrays], core_ids=[0])
    return result.results[0]["out"]
```

```python
from contextlib import ExitStack

import concourse.bass as bass
from concourse import mybir

F32 = mybir.dt.float32
F16 = mybir.dt.float16
ALU = mybir.AluOpType
ACT = mybir.ActivationFunctionType
AX = mybir.AxisListType
RMAX = bass.bass_isa.ReduceOp.max

P = 128
CH = 4
L_SCALE = 2.0 ** 15
G_TOP = 2.0 ** 14
TINY = 1e-37
TINY_SQ = 1e-30
EPS = 1e-5


def stage1_steps(B, T):
    shells = [[("a", k, j, min(j + CH, T)) for j in range(k, T, CH)] for k in range(T)]
    batches = [[("x", b * (T // CH) + c) for c in range(T // CH)] for b in range(B)]
    steps = batches[0] + batches[1]
    for k in range(T):
        batch = batches[k + 2] if k + 2 < B else []
        for i in range(max(len(batch), len(shells[k]))):
            steps += shells[k][i:i + 1] + batch[i:i + 1]
        steps.append(("r", k))
    return steps


def relu_parts(k, T):
    half, late = T // 2, 3 * T // 4
    done = [(k, 0, T, 0)] if k < half else [(k, half, T, 1)] if k < late else [(k, late, T, 2)]
    first = {half - 1: half, half: half + 2, late - 1: late, late: late + 2}.get(k)
    if first:
        done += [(row, 0, half, 0) for row in (first, first + 1)]
    if k == late - 1:
        done += [(row, half, late, 1) for row in range(late, T)]
    return done


def copy_on_dve(g):
    return g % 4 == 1


def copies_up_to(g):
    return sum(copy_on_dve(i) == copy_on_dve(g) for i in range(g + 1))


def relu_on_dve(part, row, T):
    return part >= 1 and row >= 3 * T // 4


def gnn_resnorm(nc, x, adj, W, out):
    B, N, F = x.shape
    T = N // P
    C = T // CH
    H = 2
    BH = B // H
    every = slice(0, BH)
    last_parts = [slice(0, BH - 1), slice(BH - 1, BH)]
    assert F == P and BH * F == 512 and C == 4
    NG = B * C
    XD = 2
    R = 3
    steps = stage1_steps(B, T)
    a_steps = [s for s in steps if s[0] == "a"]
    pair_of, pair_free, free = [], [], {0: 0, 1: 0}
    for i, step in enumerate(steps):
        if step[0] == "a":
            pair = len(pair_of) % 2 if ("x", NG - 1) in steps[:i] else 0
            pair_of.append(pair)
            pair_free.append(free[pair])
            free[pair] = len(pair_of)
    last_a = {s[1]: i + 1 for i, s in enumerate(a_steps)}
    NA = len(a_steps)
    relus = [part for k in range(T) for part in relu_parts(k, T) if not relu_on_dve(part[3], part[0], T)]
    group_relus = [1 + max(i for i, part in enumerate(relus) if part[0] // CH == c) for c in range(C)]
    chain_at = [sum(1 + (c * CH >= T // 2) + (c * CH >= 3 * T // 4) for c in range(n)) for n in range(C + 1)]

    x_t = x.rearrange("b (t p) f -> b p t f", p=P)
    x_n = x.rearrange("b (t p) f -> p b t f", p=P)
    out_n = out.rearrange("b (t p) f -> p b t f", p=P)
    adj_t = adj.rearrange("(t p) c -> p t c", p=P)

    with ExitStack() as ctx:
        def sb(name, shape, dt=F32):
            return ctx.enter_context(nc.sbuf_tensor(name, shape, dt))

        def sem(name):
            return ctx.enter_context(nc.semaphore(name))

        S = sb("S", [P, T, N])
        X = sb("X", [P, B, T * F])
        S16 = S[:, :, :].bitcast(F16).rearrange("p t (n s c) -> p t n s c", s=2, c=P)
        X32 = X[:, :, :].rearrange("p b (t f) -> p b t f", f=F)
        G16 = X[:, :, :].bitcast(F16).rearrange("p b (t s f) -> p b t s f", s=2, f=F)
        Wsb = sb("Wsb", [P, F])
        ident = sb("ident", [P, P])
        work = sb("work", [P, 2, CH * P])
        scaled = sb("scaled", [P, 2, CH, P])
        xo = sb("xo", [P, H, BH, F])
        Wsq = xo[:, 0, 0, :]
        ones = xo[:, 0, 1, :]
        squares = scaled[:, 0].rearrange("p b c -> p (b c)").bitcast(mybir.dt.bfloat16)
        xss = sb("xss", [P, 2, B])
        xss_sum = sb("xss_sum", [P, B])
        xall = sb("xall", [P, B])
        bound = sb("bound", [P, B])
        gscale = sb("gscale", [P, B])
        gback = sb("gback", [P, B])
        wbound = sb("wbound", [P, 2])
        rowsum = sb("rowsum", [P, 3, T])
        rowsafe = sb("rowsafe", [P, T])
        mhalf = sb("mhalf", [P, T])
        phalf = sb("phalf", [P, B])
        dinv = sb("dinv", [P, T])
        dneg = sb("dneg", [P, T])
        stats = sb("stats", [P, H, BH, 6])
        pairsum = sb("pairsum", [P, H, BH, 2])
        meandiff = sb("meandiff", [P, H, BH])
        diffsq = sb("diffsq", [P, H, BH])
        vareps = sb("vareps", [P, H, BH])
        negmean = sb("negmean", [P, H, BH])
        rstd = sb("rstd", [P, H, BH])
        shift = sb("shift", [P, H, BH])

        psum = ctx.enter_context(nc.psum_tensor("psum", [P, 8 * 512], F32))
        bank = [psum[:, i * 512:(i + 1) * 512] for i in range(8)]
        xT_ps = bank[0:R]
        G_ps = bank[R:2 * R]
        at_ps = [bank[6:8], bank[2:4]]
        dB = psum[:, 0:T * P]
        acc = [bank[4], bank[5]]
        xT_sb = [work[:, 0, :], work[:, 1, :], scaled[:, 1].rearrange("p a b -> p (a b)")]

        x0_in = [sem(f"x0_in{c}") for c in range(C)]
        x_in = [None] + [sem(f"x_in{b}") for b in range(1, B)]
        shell_in = [sem(f"shell_in{k}") for k in range(T)]
        w_in = sem("w_in")
        consts = sem("consts")
        wsq_done = sem("wsq_done")
        wsum = sem("wsum")
        wb_ready = sem("wb_ready")
        xss_ready = sem("xss_ready")
        xss_sum_ready = sem("xss_sum_ready")
        xall_ready = sem("xall_ready")
        bound_ready = sem("bound_ready")
        gscale_ready = sem("gscale_ready")
        groot_ready = sem("groot_ready")
        gback_ready = sem("gback_ready")
        xT_ready = sem("xT_ready")
        xT_copied = {False: sem("xT_copied_act"), True: sem("xT_copied_dve")}
        g_ready = sem("g_ready")
        ghi_done = sem("ghi_done")
        glo_done = sem("glo_done")
        at_ready = sem("at_ready")
        adds_done = sem("adds_done")
        relu_act = sem("relu_act")
        relu_dve = sem("relu_dve")
        rs_chain = sem("rs_chain")
        rowsafe_ready = sem("rowsafe_ready")
        d_ready = sem("d_ready")
        dneg_ready = sem("dneg_ready")
        dB_ready = sem("dB_ready")
        scaled_ready = sem("scaled_ready")
        shi_done = sem("shi_done")
        slo_done = sem("slo_done")
        acc_ready = sem("acc_ready")
        acc_read = [sem(f"acc_read{h}") for h in range(H)]
        gn_ready = sem("gn_ready")
        branch_ready = sem("branch_ready")
        xo_in = [sem(f"xo_in{h}") for h in range(H)]
        r_ready = sem("r_ready")
        stats_done = sem("stats_done")
        pairs_done = sem("pairs_done")
        var_ready = sem("var_ready")
        ve_done = sem("ve_done")
        rstd_done = sem("rstd_done")
        shift_ready = sem("shift_ready")
        last_out = sem("last_out")
        out_ready = sem("out_ready")
        stored = [sem(f"stored{h}") for h in range(H)]

        block = ctx.enter_context(nc.Block())

        def squares_inputs(eng, b, half):
            for s in x0_in[half * C // 2:(half + 1) * C // 2] if b == 0 else [x_in[b]]:
                eng.wait_ge(s, 16)
            if 2 * b + half:
                eng.wait_ge(xss_ready, 2 * b + half)
            return X[:, b, half * T // 2 * F:(half + 1) * T // 2 * F]

        @block.sync
        def _(sp):
            for c in range(C):
                sp.dma_start(X32[:, 0, c * CH:(c + 1) * CH], x_t[0][:, c * CH:(c + 1) * CH])\
                  .then_inc(x0_in[c], 16)
                if c == 0:
                    sp.dma_start(Wsb[:, :], W).then_inc(w_in, 16)
            sp.dma_start(X32[:, 1], x_t[1]).then_inc(x_in[1], 16)
            for k in range(T):
                sp.dma_start(S[:, k, k * P:], adj_t[:, k, k * P:]).then_inc(shell_in[k], 16)
                if k + 1 < T:
                    sp.dma_start(S[:, k + 1:, k * P:(k + 1) * P],
                                 adj_t[:, k + 1:, k * P:(k + 1) * P]).then_inc(shell_in[k], 16)
                if k + 2 < B:
                    sp.dma_start(X32[:, k + 2], x_t[k + 2]).then_inc(x_in[k + 2], 16)
            sp.wait_ge(wb_ready, 1)
            for h in range(H):
                sp.dma_start(xo[:, h], x_n[:, h * BH:(h + 1) * BH, 0]).then_inc(xo_in[h], 16)

            def store(n, h, bs=every):
                sp.dma_start(out_n[:, h * BH + bs.start:h * BH + bs.stop, bass.ds(n, 1)]
                             .rearrange("p b t f -> p b (t f)"), xo[:, h, bs]).then_inc(stored[h], 16)

            with sp.Fori(0, T - 1) as n:
                for h in range(H):
                    sp.wait_ge(out_ready, H * n + h + 1)
                    store(n, h)
                for h in range(H):
                    sp.wait_ge(stored[h], 16 * n + 16)
                    sp.dma_start(xo[:, h], x_n[:, h * BH:(h + 1) * BH, bass.ds(n + 1, 1)].rearrange("p b t f -> p b (t f)"))\
                      .then_inc(xo_in[h], 16)
            sp.wait_ge(out_ready, H * T - 1)
            store(T - 1, 0)
            sp.wait_ge(out_ready, H * T)
            store(T - 1, 1, last_parts[0])
            sp.wait_ge(last_out, 1)
            store(T - 1, 1, last_parts[1])
            sp.wait_ge(stored[0], 16 * T)
            sp.wait_ge(stored[1], 16 * T + 16)

        @block.gpsimd
        def _(pool):
            pool.memset(ident[:, :], 0.0).then_inc(consts, 1)
            pool.memset(ones, 1.0).then_inc(consts, 1)
            pool.memset(mhalf[:, :], -0.5).then_inc(consts, 1)
            pool.memset(phalf[:, :], 0.5).then_inc(consts, 1)
            pool.wait_ge(consts, 1)
            pool.affine_select(out=ident[:, :], in_=ident[:, :], compare_op=ALU.not_equal, fill=1.0,
                               base=0, pattern=[[-1, P]], channel_multiplier=1).then_inc(consts, 1)
            pool.wait_ge(consts, 5)

            def batch_bound(b):
                pool.wait_ge(xss_ready, 2 * b + 2)
                pool.tensor_tensor(xss_sum[:, b:b + 1], xss[:, 0, b:b + 1], xss[:, 1, b:b + 1], ALU.add)\
                    .then_inc(xss_sum_ready, 1)
                pool.wait_ge(xss_sum_ready, b + 1)
                pool.partition_all_reduce(xall[:, b:b + 1], xss_sum[:, b:b + 1], P, RMAX).then_inc(xall_ready, 1)
                pool.wait_ge(xall_ready, b + 1)
                if b == 0:
                    pool.wait_ge(wb_ready, 1)
                pool.tensor_scalar(bound[:, b:b + 1], xall[:, b:b + 1], wbound[:, 1:2], TINY_SQ,
                                   ALU.mult, ALU.max).then_inc(bound_ready, 1)
                pool.wait_ge(bound_ready, b + 1)
                pool.tensor_tensor(gscale[:, b:b + 1], bound[:, b:b + 1], mhalf[:, 0:1], ALU.pow)\
                    .then_inc(gscale_ready, 1)

            def row_scales(c):
                g = slice(c * CH, (c + 1) * CH)
                late = (c + 1) * CH > 3 * T // 4
                pool.wait_ge(relu_act, group_relus[c])
                pool.tensor_scalar(rowsafe[:, g], rowsum[:, 0, g], TINY, 1.0, ALU.add, ALU.mult)\
                    .then_inc(rs_chain, 1)
                for part in range(1, 1 + (c * CH >= T // 2) + late):
                    pool.wait_ge(rs_chain, chain_at[c] + part)
                    if late:
                        pool.wait_ge(relu_dve, CH * part)
                    pool.tensor_tensor(rowsafe[:, g], rowsafe[:, g], rowsum[:, part, g], ALU.add)\
                        .then_inc(rs_chain, 1)
                pool.wait_ge(rs_chain, chain_at[c + 1])
                pool.tensor_tensor(dinv[:, g], rowsafe[:, g], mhalf[:, 0:CH], ALU.pow).then_inc(d_ready, 1)
                pool.wait_ge(d_ready, c + 1)
                pool.tensor_scalar(dneg[:, g], dinv[:, g], -L_SCALE, 0.0, ALU.mult, ALU.add)\
                    .then_inc(dneg_ready, 1)

            for b in range(B):
                batch_bound(b)
            pool.tensor_tensor(gback[:, :], bound[:, :], phalf[:, :], ALU.pow).then_inc(groot_ready, 1)
            pool.wait_ge(groot_ready, 1)
            pool.tensor_scalar(gback[:, :], gback[:, :], 1.0 / L_SCALE, 0.0, ALU.mult, ALU.add)\
                .then_inc(gback_ready, 1)
            for c in range(C):
                row_scales(c)

            def scale_and_shift(h, count, bs=every):
                pool.wait_ge(var_ready, count)
                pool.tensor_tensor(rstd[:, h, bs], vareps[:, h, bs], mhalf[:, bs], ALU.pow)\
                    .then_inc(rstd_done, 1)
                pool.wait_ge(rstd_done, count)
                pool.tensor_tensor(shift[:, h, bs], negmean[:, h, bs], rstd[:, h, bs], ALU.mult)\
                    .then_inc(shift_ready, 1)

            with pool.Fori(0, T - 1) as n:
                for h in range(H):
                    scale_and_shift(h, n * H + h + 1)
            scale_and_shift(0, T * H - 1)
            for i, bs in enumerate(last_parts):
                scale_and_shift(1, T * H + i, bs)

        @block.scalar
        def _(act):
            def x_transposed(g):
                act.wait_ge(xT_ready, g + 1)
                if g >= R:
                    act.wait_ge(g_ready, g - R + 1)
                act.copy(xT_sb[g % R], xT_ps[g % R]).then_inc(xT_copied[False], 1)

            def x_squares(b, half):
                x_half = squares_inputs(act, b, half)
                act.activation(squares, x_half, ACT.Square, accum_out=xss[:, half, b:b + 1])\
                   .then_inc(xss_ready, 1)

            def g_hi(g):
                b, c = divmod(g, C)
                act.wait_ge(g_ready, g + 1)
                act.wait_ge(gscale_ready, b + 1)
                act.activation(G16[:, b, c * CH:(c + 1) * CH, 0, :],
                               G_ps[g % R].rearrange("p (t f) -> p t f", f=F),
                               ACT.Copy, scale=gscale[:, b:b + 1]).then_inc(ghi_done, 1)

            def s_hi(n, c):
                act.wait_ge(scaled_ready, n * C + c + 1)
                act.copy(S16[:, c * CH:(c + 1) * CH, bass.ds(n, 1), 0, :].rearrange("p t n c -> p t (n c)"),
                         scaled[:, c % 2]).then_inc(shi_done, 1)

            hi_at = {T // 2 - 1: 0, T // 2: 1}
            hi_after = {T - 4: 2, T - 1: 3}
            for step in steps:
                if step[0] == "x":
                    g = step[1]
                    if not copy_on_dve(g):
                        x_transposed(g)
                    if g >= 1:
                        g_hi(g - 1)
                    if g % C in (1, 2) and XD <= g // C + 1 < B:
                        x_squares(g // C + 1, g % C - 1)
                    if g == NG - 1:
                        g_hi(g)
                elif step[0] == "r":
                    act.wait_ge(adds_done, last_a[step[1]])
                    for i, (row, j0, j1, part) in enumerate(relu_parts(step[1], T)):
                        if i == 1 and step[1] in hi_at:
                            s_hi(0, hi_at[step[1]])
                        if not relu_on_dve(part, row, T):
                            act.activation(S[:, row, j0 * P:j1 * P], S[:, row, j0 * P:j1 * P], ACT.Relu,
                                           accum_out=rowsum[:, part, row:row + 1]).then_inc(relu_act, 1)
                    if step[1] in hi_after:
                        s_hi(0, hi_after[step[1]])

            def normalize(n, h, bs=every):
                act.wait_ge(shift_ready, n * H + h + 1)
                for b in range(bs.start, bs.stop):
                    last = act.activation(xo[:, h, b, :], xo[:, h, b, :], ACT.Identity,
                                          scale=rstd[:, h, b:b + 1], bias=shift[:, h, b:b + 1])
                last.then_inc(out_ready, 1)

            with act.Fori(0, T - 1) as n:
                for c in range(C):
                    s_hi(n + 1, c)
                for h in range(H):
                    normalize(n, h)
            normalize(T - 1, 0)
            normalize(T - 1, 1, last_parts[0])

        @block.vector
        def _(dve):
            dve.wait_ge(w_in, 16)
            dve.tensor_tensor(Wsq, Wsb[:, :], Wsb[:, :], ALU.mult).then_inc(wsq_done, 1)
            dve.wait_ge(wsum, 1)
            dve.tensor_reduce(wbound[:, 0:1], G_ps[2][:, 0:F], AX.X, ALU.max).then_inc(wsq_done, 1)
            dve.wait_ge(wsq_done, 2)
            dve.tensor_scalar(wbound[:, 1:2], wbound[:, 0:1], G_TOP ** -2, None, ALU.mult).then_inc(wb_ready, 1)

            def x_transposed(g):
                dve.wait_ge(xT_ready, g + 1)
                if g >= R:
                    dve.wait_ge(g_ready, g - R + 1)
                dve.tensor_copy(xT_sb[g % R], xT_ps[g % R]).then_inc(xT_copied[True], 1)

            def x_squares(b, half):
                x_half = squares_inputs(dve, b, half)
                dve.scalar_tensor_tensor(out=squares, in0=x_half, scalar=1.0, in1=x_half,
                                         op0=ALU.mult, op1=ALU.mult,
                                         accum_out=xss[:, half, b:b + 1]).then_inc(xss_ready, 1)

            def g_lo(g):
                b, c = divmod(g, C)
                dve.wait_ge(ghi_done, g + 1)
                dve.wait_ge(gscale_ready, b + 1)
                dve.scalar_tensor_tensor(out=G16[:, b, c * CH:(c + 1) * CH, 1, :],
                                         in0=G_ps[g % R].rearrange("p (t f) -> p t f", f=F),
                                         scalar=gscale[:, b:b + 1],
                                         in1=G16[:, b, c * CH:(c + 1) * CH, 0, :],
                                         op0=ALU.mult, op1=ALU.subtract).then_inc(glo_done, 1)

            def s_scale(n, c, first):
                if first:
                    dve.wait_ge(d_ready, c + 1)
                    dve.wait_ge(dB_ready, 1)
                if c >= 2 or not first:
                    dve.wait_ge(slo_done, n * C + (c - 1))
                for i in range(CH):
                    m = c * CH + i
                    last = dve.scalar_tensor_tensor(out=scaled[:, c % 2, i, :], in0=S[:, m, bass.ts(n, P)],
                                                    scalar=dinv[:, m:m + 1], in1=dB[:, bass.ts(n, P)],
                                                    op0=ALU.mult, op1=ALU.mult)
                last.then_inc(scaled_ready, 1)

            def s_lo(n, c):
                dve.wait_ge(shi_done, n * C + c + 1)
                tiles = S16[:, c * CH:(c + 1) * CH, bass.ds(n, 1), :, :].rearrange("p t n s c -> p t (n s) c")
                dve.tensor_tensor(tiles[:, :, 1, :], scaled[:, c % 2], tiles[:, :, 0, :], ALU.subtract)\
                   .then_inc(slo_done, 1)

            def s_split(n):
                for c in range(C):
                    s_scale(n, c, first=False)
                    if c:
                        s_lo(n, c - 1)
                s_lo(n, C - 1)

            scale_after = {T // 2 - 1: 0, T // 2: 1, T - 4: 2, T - 1: 3}
            lo_after = {T // 2: 0, T // 2 + 1: 1, T - 3: 2}
            na = 0
            for step in steps:
                if step[0] == "x":
                    g = step[1]
                    if g >= 2:
                        g_lo(g - 2)
                    if copy_on_dve(g):
                        x_transposed(g)
                    if g % 2 == 0 and g < 2 * XD:
                        for half in range(2):
                            x_squares(g // 2, half)
                    if g == NG - 1:
                        g_lo(g - 1)
                        g_lo(g)
                elif step[0] == "r":
                    k = step[1]
                    for row, j0, j1, part in relu_parts(k, T):
                        if relu_on_dve(part, row, T):
                            dve.wait_ge(adds_done, last_a[k])
                            tiles = S[:, row, j0 * P:j1 * P]
                            dve.scalar_tensor_tensor(out=tiles, in0=tiles, scalar=0.0, in1=tiles,
                                                     op0=ALU.max, op1=ALU.max,
                                                     accum_out=rowsum[:, part, row:row + 1]).then_inc(relu_dve, 1)
                    if k in lo_after:
                        s_lo(0, lo_after[k])
                    if k in scale_after:
                        s_scale(0, scale_after[k], first=True)
                else:
                    _, k, j0, j1 = step
                    pair = at_ps[pair_of[na]]
                    na += 1
                    dve.wait_ge(at_ready, na)
                    row = S[:, k, j0 * P:j1 * P]
                    last = dve.tensor_tensor(row, row, pair[0][:, 0:(j1 - j0) * P], ALU.add)
                    i0 = max(j0, k + 1)
                    if i0 < j1:
                        col = S[:, i0:j1, k * P:(k + 1) * P]
                        last = dve.tensor_tensor(
                            col, col, pair[1][:, (i0 - j0) * P:(j1 - j0) * P]
                            .rearrange("p (t c) -> p t c", c=P), ALU.add)
                    last.then_inc(adds_done, 1)

            def gather(n, h, bs=every, part=0):
                i = n * H + h + part
                t = work[:, h, :].rearrange("p (b f) -> p b f", f=F)[:, bs]
                Gn = G16[:, h * BH + bs.start:h * BH + bs.stop, bass.ds(n, 1), :, :].rearrange("p b t s f -> p b (t s) f")
                dve.tensor_tensor(t, Gn[:, :, 0, :], Gn[:, :, 1, :], ALU.add).then_inc(gn_ready, 1)
                dve.wait_ge(gn_ready, i + 1)
                dve.wait_ge(acc_ready, i + 1)
                dve.scalar_tensor_tensor(out=t, in0=t, scalar=L_SCALE,
                                         in1=acc[h - part][:, 0:(bs.stop - bs.start) * F]
                                         .rearrange("p (b f) -> p b f", f=F),
                                         op0=ALU.mult, op1=ALU.add).then_inc(acc_read[h], 1)

            def statistics(n, h, bs=every, part=0):
                i = n * H + h + part
                t = work[:, h, :].rearrange("p (b f) -> p b f", f=F)[:, bs]
                dve.wait_ge(acc_read[h], n + 1 + part)
                back = gback[:, h * BH + bs.start:h * BH + bs.stop].rearrange("p (b o) -> p b o", o=1)\
                    .broadcast_to([P, bs.stop - bs.start, F])
                dve.scalar_tensor_tensor(out=t, in0=t, scalar=0.0, in1=back,
                                         op0=ALU.max, op1=ALU.mult).then_inc(branch_ready, 1)
                dve.wait_ge(branch_ready, i + 1)
                dve.wait_ge(xo_in[h], n * 16 + 16)
                dve.tensor_tensor(xo[:, h, bs], t, xo[:, h, bs], ALU.add).then_inc(r_ready, 1)
                dve.wait_ge(r_ready, i + 1)
                for b in range(bs.start, bs.stop):
                    last = dve.bn_stats(stats[:, h, b, :], xo[:, h, b, :])
                last.then_inc(stats_done, 1)
                dve.wait_ge(stats_done, i + 1)
                dve.tensor_tensor(pairsum[:, h, bs], stats[:, h, bs, 1:3], stats[:, h, bs, 4:6], ALU.add)
                dve.tensor_tensor(meandiff[:, h, bs], stats[:, h, bs, 1], stats[:, h, bs, 4], ALU.subtract)\
                   .then_inc(pairs_done, 1)
                dve.wait_ge(pairs_done, i + 1)
                dve.scalar_tensor_tensor(out=diffsq[:, h, bs], in0=meandiff[:, h, bs], scalar=0.25,
                                         in1=meandiff[:, h, bs], op0=ALU.mult, op1=ALU.mult)
                dve.tensor_scalar(vareps[:, h, bs], pairsum[:, h, bs, 1], 1.0 / F, EPS, ALU.mult, ALU.add)\
                   .then_inc(ve_done, 1)
                dve.tensor_scalar(negmean[:, h, bs], pairsum[:, h, bs, 0], -0.5, None, ALU.mult)
                dve.wait_ge(ve_done, i + 1)
                dve.tensor_tensor(vareps[:, h, bs], vareps[:, h, bs], diffsq[:, h, bs], ALU.add)\
                   .then_inc(var_ready, 1)

            s_lo(0, C - 1)
            for c in range(C):
                s_scale(1, c, first=False)
                if c:
                    s_lo(1, c - 1)
                if c >= C - H:
                    gather(0, c - (C - H))
            s_lo(1, C - 1)
            dve.wait_ge(gback_ready, 1)
            for h in range(H):
                statistics(0, h)
            dve.wait_ge(dB_ready, C)
            with dve.Fori(1, T - 1) as n:
                s_split(n + 1)
                for h in range(H):
                    gather(n, h)
                    statistics(n, h)
            gather(T - 1, 0)
            statistics(T - 1, 0)
            for part, bs in enumerate(last_parts):
                gather(T - 1, 1, bs, part)
                statistics(T - 1, 1, bs, part)
            dve.wait_ge(shift_ready, T * H + 1)
            for b in range(last_parts[1].start, BH):
                last = dve.tensor_scalar(xo[:, 1, b, :], xo[:, 1, b, :], rstd[:, 1, b:b + 1],
                                         shift[:, 1, b:b + 1], ALU.mult, ALU.add)
            last.then_inc(last_out, 1)

        @block.tensor
        def _(pe):
            pe.wait_ge(consts, 5)
            pe.wait_ge(wsq_done, 1)
            pe.matmul(G_ps[2][:, 0:F], ones, Wsq, start=True, stop=True)\
              .then_inc(wsum, 1)

            def x_transposes(g):
                b, c = divmod(g, C)
                if b == 0:
                    pe.wait_ge(x0_in[c], 16)
                elif c == 0:
                    pe.wait_ge(x_in[b], 16)
                if g >= R:
                    pe.wait_ge(xT_copied[copy_on_dve(g - R)], copies_up_to(g - R))
                for i in range(CH):
                    last = pe.transpose(xT_ps[g % R][:, i * P:(i + 1) * P], X32[:, b, c * CH + i, :], ident[:, :])
                last.then_inc(xT_ready, 1)

            def x_times_w(g):
                pe.wait_ge(xT_copied[copy_on_dve(g)], copies_up_to(g))
                if g == 2:
                    pe.wait_ge(wb_ready, 1)
                if g >= R:
                    pe.wait_ge(glo_done, g - R + 1)
                for i in range(CH):
                    last = pe.matmul(G_ps[g % R][:, i * F:(i + 1) * F], xT_sb[g % R][:, i * P:(i + 1) * P],
                                     Wsb[:, :], start=True, stop=True)
                last.then_inc(g_ready, 1)

            def d_columns(c):
                pe.wait_ge(dneg_ready, c + 1)
                if c == 0:
                    pe.wait_ge(glo_done, NG)
                if c == 2:
                    pe.wait_ge(adds_done, NA)
                for n in range(c * CH, (c + 1) * CH):
                    last = pe.transpose(dB[:, n * P:(n + 1) * P], dneg[:, n:n + 1].broadcast_to([P, P]), ident[:, :])
                last.then_inc(dB_ready, 1)

            def three_products(n, m, h, bs=every, part=0):
                Lm = S16[:, m, bass.ds(n, 1), :, :].rearrange("p n s c -> p (n s) c")
                Gm = G16[:, h * BH + bs.start:h * BH + bs.stop, m, :, :]
                out = acc[h - part][:, 0:(bs.stop - bs.start) * F]
                for i, (ls, gs) in enumerate(((0, 0), (0, 1), (1, 0))):
                    last = pe.matmul(out, Lm[:, ls, :], Gm[:, :, gs, :],
                                     start=(m == 0 and i == 0), stop=(m == T - 1 and i == 2))
                if m == T - 1:
                    last.then_inc(acc_ready, 1)

            def first_products(m):
                if m % CH == 0:
                    pe.wait_ge(slo_done, m // CH + 1)
                for h in range(H):
                    three_products(0, m, h)

            first_from = [T // 2 + 1] * (T // 2) + [T] * (T // 2)
            early = list(range(T))
            dB_after = {T // 2 - 2: 0, T // 2 + 1: 1}
            na = 0
            for step in steps:
                if step[0] == "x":
                    g = step[1]
                    x_transposes(g)
                    if g >= 1:
                        x_times_w(g - 1)
                    if g == NG - 1:
                        x_times_w(g)
                elif step[0] == "r":
                    if step[1] in dB_after:
                        d_columns(dB_after[step[1]])
                else:
                    _, k, j0, j1 = step
                    pair = at_ps[pair_of[na]]
                    if j0 == k:
                        pe.wait_ge(shell_in[k], 32 if k + 1 < T else 16)
                    if pair_free[na]:
                        pe.wait_ge(adds_done, pair_free[na])
                    if pair_of[na] == 1:
                        pe.wait_ge(glo_done, NG)
                    na += 1
                    for j in range(j0, j1):
                        at = slice((j - j0) * P, (j - j0 + 1) * P)
                        last = pe.transpose(pair[0][:, at], S[:, j, k * P:(k + 1) * P], ident[:, :])
                        if j > k:
                            last = pe.transpose(pair[1][:, at], S[:, k, j * P:(j + 1) * P], ident[:, :])
                    last.then_inc(at_ready, 1)
                    if k >= first_from[T - len(early)]:
                        first_products(early.pop(0))

            while len(early) > CH:
                first_products(early.pop(0))
            d_columns(2)
            d_columns(3)
            pe.wait_ge(slo_done, C)
            for h in range(H):
                for m in early:
                    three_products(0, m, h)

            def products(n, halves=range(H)):
                for h in halves:
                    pe.wait_ge(acc_read[h], n)
                    for m in range(T):
                        if h == 0 and m % CH == 0:
                            pe.wait_ge(slo_done, n * C + (m // CH + 1))
                        three_products(n, m, h)

            with pe.Fori(1, T - 1) as n:
                products(n)
            products(T - 1, halves=[0])
            for part, bs in enumerate(last_parts):
                pe.wait_ge(acc_read[1 - part], T - 1 + part)
                for m in range(T):
                    three_products(T - 1, m, 1, bs, part)


def kernel(x, adj, L0_gnn_W):
    import numpy as np
    import concourse.bacc as bacc
    from concourse.bass_utils import run_bass_kernel_spmd

    nc = bacc.Bacc("TRN2", target_bir_lowering=False, num_devices=1)
    arrays, aps = {}, []
    for name, a in (("x", x), ("adj", adj), ("W", L0_gnn_W)):
        a = np.ascontiguousarray(a)
        arrays[f"in_{name}"] = a
        aps.append(nc.dram_tensor(f"in_{name}", a.shape, mybir.dt.from_np(a.dtype), kind="ExternalInput").ap())
    out = nc.dram_tensor("out", x.shape, F32, kind="ExternalOutput").ap()
    gnn_resnorm(nc, *aps, out)
    result = run_bass_kernel_spmd(nc, [arrays], core_ids=[0])
    return result.results[0]["out"]
```
